# Optimizing a Trainium2 kernel written in Bass

```python
import numpy as np
import jax
import jax.numpy as jnp

def _softmax(x, axis=-1):
    return jax.nn.softmax(x, axis=axis)

def _gelu(x):
    return jax.nn.gelu(x, approximate=True)

def _silu(x):
    return jax.nn.silu(x)

def _sigmoid(x):
    return jax.nn.sigmoid(x)

def _layernorm(x, axis=-1, eps=1e-05):
    m = jnp.mean(x, axis=axis, keepdims=True)
    v = jnp.var(x, axis=axis, keepdims=True)
    return (x - m) / jnp.sqrt(v + eps)

def _scatter_add(tgt, idx, src, axis=0):
    return tgt.at[idx].add(src)

def _segment_sum(src, seg, n):
    return jax.ops.segment_sum(src, seg, n)
kernel_name = 'mk_cond_resid_d4_seqx_r8_b2f14b'

def setup_inputs(seed: int=0):
    np.random.seed(seed)
    _w = jnp.asarray

    def _rec_inputs():
        import jax
        import jax.numpy as jnp
        _rk = jax.random.key(seed)
        x = -7.109e-05 + 0.9999 * jax.random.normal(jax.random.fold_in(_rk, 1), (32, 32, 256), jnp.float32)
        _lenS = 32 - jax.random.randint(jax.random.fold_in(_rk, 7), (32,), 0, max(1, 32 // 4) + 1, jnp.int32)
        _lenS2 = 32 - jax.random.randint(jax.random.fold_in(_rk, 8), (32,), 0, max(1, 32 // 4) + 1, jnp.int32)
        itok_B_1_198 = jax.random.randint(jax.random.fold_in(_rk, 11), (32,), 1, 199, jnp.int32)
        itok_B_0_3 = jax.random.randint(jax.random.fold_in(_rk, 12), (32,), 0, 4, jnp.int32)
        itok_B_0_6 = jax.random.randint(jax.random.fold_in(_rk, 13), (32,), 0, 7, jnp.int32)
        itok_B_0_15 = jax.random.randint(jax.random.fold_in(_rk, 14), (32,), 0, 16, jnp.int32)
        return (x, itok_B_1_198, itok_B_0_3, itok_B_0_6, itok_B_0_15)
    x, itok_B_1_198, itok_B_0_3, itok_B_0_6, itok_B_0_15 = _rec_inputs()

    def _L0_cond_setup():
        import jax, jax.numpy as jnp
        import numpy as np
        B, C, T = (128, 32, 256)
        S, D = (200, 32)
        key = jax.random.key(seed)
        k1, k2, k3 = jax.random.split(key, 3)
        x = jax.random.normal(k1, (B, C, T), dtype=jnp.float32)
        conditions = jax.random.randint(k2, (B,), 0, S, dtype=jnp.int64)
        weights = jax.random.normal(k3, (S, C, D), dtype=jnp.float32) / jnp.sqrt(jnp.float32(C))
        return {'x': x, 'conditions': conditions, 'weights': weights}
    _L0_cond_all = _L0_cond_setup()
    _L0_cond_in = {k: v for k, v in _L0_cond_all.items() if k in ('weights',)}
    del _L0_cond_all

    def _L1_cond_setup():
        import jax, jax.numpy as jnp
        import numpy as np
        B, S, D_IN, D_OUT, R, E = (8, 256, 256, 256, 16, 4)
        key = jax.random.key(seed)
        ks = jax.random.split(key, 7)
        x = jax.random.normal(ks[0], (B, S, D_IN), dtype=jnp.float32)
        W_base = jax.random.normal(ks[1], (D_OUT, D_IN), dtype=jnp.float32) * 0.02
        Wt = jax.random.normal(ks[2], (D_IN, D_IN), dtype=jnp.float32) * 0.02
        A = jax.random.normal(ks[3], (E, R, D_IN), dtype=jnp.float32) * 0.02
        B_w = jax.random.normal(ks[4], (E, D_OUT, R), dtype=jnp.float32) * 0.02
        Wp = jax.random.normal(ks[5], (D_OUT, D_OUT), dtype=jnp.float32) * 0.02
        scaling = jnp.ones((E,), dtype=jnp.float32)
        adapter_idx = jax.random.randint(ks[6], (B,), 0, E)
        return {'x': x, 'W_base': W_base, 'Wt': Wt, 'A': A, 'B_w': B_w, 'Wp': Wp, 'scaling': scaling, 'adapter_idx': adapter_idx}
    _L1_cond_all = _L1_cond_setup()
    _L1_cond_in = {k: v for k, v in _L1_cond_all.items() if k in ('W_base', 'Wt', 'A', 'B_w', 'Wp', 'scaling')}
    del _L1_cond_all

    def _L2_cond_setup():
        import jax, jax.numpy as jnp
        import numpy as np
        B, T, D_IN, D_OUT = (16, 256, 256, 256)
        N_ADAPTERS, RANK = (8, 16)
        key = jax.random.key(seed)
        k_x, k_w, k_a, k_b, k_s, k_idx = jax.random.split(key, 6)
        x = jax.random.normal(k_x, (B, T, D_IN), dtype=jnp.float32)
        W = jax.random.normal(k_w, (D_OUT, D_IN), dtype=jnp.float32) * (1.0 / np.sqrt(D_IN))
        A = jax.random.normal(k_a, (N_ADAPTERS, RANK, D_IN), dtype=jnp.float32) * 0.02
        Bm = jax.random.normal(k_b, (N_ADAPTERS, D_OUT, RANK), dtype=jnp.float32) * 0.02
        scalings = jnp.ones((N_ADAPTERS,), dtype=jnp.float32)
        adapter_idx = jax.random.randint(k_idx, (B,), 0, N_ADAPTERS, dtype=jnp.int32)
        return {'x': x, 'W': W, 'A': A, 'Bm': Bm, 'scalings': scalings, 'adapter_idx': adapter_idx}
    _L2_cond_all = _L2_cond_setup()
    _L2_cond_in = {k: v for k, v in _L2_cond_all.items() if k in ('W', 'A', 'Bm', 'scalings')}
    del _L2_cond_all

    def _L3_cond_setup():
        import jax, jax.numpy as jnp
        import numpy as np
        key = jax.random.key(seed)
        k1, k2, k3, k4 = jax.random.split(key, 4)
        B, S, IN, OUT, E = (64, 32, 256, 256, 16)
        bound = 1.0 / np.sqrt(IN)
        x = jax.random.normal(k1, (B, S, IN), dtype=jnp.float32)
        idx = jax.random.randint(k2, (B,), 0, E, dtype=jnp.int64)
        W = jax.random.uniform(k3, (E, IN, OUT), dtype=jnp.float32, minval=-bound, maxval=bound)
        b = jnp.full((E, OUT), 0.1, dtype=jnp.float32)
        return {'x': x, 'id': idx, 'W': W, 'b': b}
    _L3_cond_all = _L3_cond_setup()
    _L3_cond_in = {k: v for k, v in _L3_cond_all.items() if k in ('W', 'b')}
    del _L3_cond_all
    return {'x': x, 'itok_B_1_198': itok_B_1_198, 'itok_B_0_3': itok_B_0_3, 'itok_B_0_6': itok_B_0_6, 'itok_B_0_15': itok_B_0_15, 'L0_cond_weights': _L0_cond_in['weights'], 'L1_cond_W_base': _L1_cond_in['W_base'], 'L1_cond_Wt': _L1_cond_in['Wt'], 'L1_cond_A': _L1_cond_in['A'], 'L1_cond_B_w': _L1_cond_in['B_w'], 'L1_cond_Wp': _L1_cond_in['Wp'], 'L1_cond_scaling': _L1_cond_in['scaling'], 'L2_cond_W': _L2_cond_in['W'], 'L2_cond_A': _L2_cond_in['A'], 'L2_cond_Bm': _L2_cond_in['Bm'], 'L2_cond_scalings': _L2_cond_in['scalings'], 'L3_cond_W': _L3_cond_in['W'], 'L3_cond_b': _L3_cond_in['b']}

def reference(x, itok_B_1_198, itok_B_0_3, itok_B_0_6, itok_B_0_15, L0_cond_weights, L1_cond_W_base, L1_cond_Wt, L1_cond_A, L1_cond_B_w, L1_cond_Wp, L1_cond_scaling, L2_cond_W, L2_cond_A, L2_cond_Bm, L2_cond_scalings, L3_cond_W, L3_cond_b):
    import jax
    import jax.numpy as jnp

    def _L0_cond_ref(x, conditions, weights):
        import jax, jax.numpy as jnp
        import numpy as np
        B, C, T = (128, 32, 256)
        S, D = (200, 32)
        w = weights[conditions]
        return jnp.einsum('bct,bcd->bdt', x, w)

    def _L1_cond_ref(x, W_base, Wt, A, B_w, Wp, scaling, adapter_idx):
        import jax, jax.numpy as jnp
        import numpy as np
        B, S, D_IN, D_OUT, R, E = (8, 256, 256, 256, 16, 4)
        base = jnp.einsum('bsi,oi->bso', x, W_base)
        h = jnp.einsum('bsi,ji->bsj', x, Wt)
        Ab = A[adapter_idx]
        Bb = B_w[adapter_idx]
        sc = scaling[adapter_idx]
        z = jnp.einsum('bsj,brj->bsr', h, Ab)
        l = jnp.einsum('bsr,bor->bso', z, Bb)
        lora_out = jnp.einsum('bso,po->bsp', l, Wp) * sc[:, None, None]
        return base + lora_out

    def _L2_cond_ref(x, W, A, Bm, scalings, adapter_idx):
        import jax, jax.numpy as jnp
        import numpy as np
        B, T, D_IN, D_OUT = (16, 256, 256, 256)
        N_ADAPTERS, RANK = (8, 16)
        H = jnp.einsum('btd,od->bto', x, W)
        A_b = A[adapter_idx]
        B_b = Bm[adapter_idx]
        s_b = scalings[adapter_idx]
        xa = jnp.einsum('btd,brd->btr', x, A_b)
        delta = jnp.einsum('btr,bor->bto', xa, B_b)
        delta = jax.lax.stop_gradient(delta * s_b[:, None, None])
        return H + delta

    def _L3_cond_ref(x, id, W, b):
        import jax, jax.numpy as jnp
        import numpy as np
        Wg = W[id]
        bg = b[id]
        out = jnp.einsum('bsi,bio->bso', x, Wg) + bg[:, None, :]
        return out
    x = x + _L0_cond_ref(x, itok_B_1_198, L0_cond_weights)
    x = x + _L1_cond_ref(x, L1_cond_W_base, L1_cond_Wt, L1_cond_A, L1_cond_B_w, L1_cond_Wp, L1_cond_scaling, itok_B_0_3)
    x = x + _L2_cond_ref(x, L2_cond_W, L2_cond_A, L2_cond_Bm, L2_cond_scalings, itok_B_0_6)
    x = x + _L3_cond_ref(x, itok_B_0_15, L3_cond_W, L3_cond_b)
    return x

_drawn_inputs = setup_inputs


def setup_inputs(seed=0):
    import zlib

    import numpy as np

    out = dict(_drawn_inputs(seed))
    spreads = {'L1_cond_scaling': (1.0, 0.6),
     'L2_cond_scalings': (1.0, 0.6),
     'L3_cond_b': (0.10000000149011612, 0.6)}
    factors = {'L1_cond_Wt': 8.0,
     'L1_cond_A': 8.0,
     'L1_cond_B_w': 8.0,
     'L1_cond_Wp': 8.0,
     'L2_cond_A': 3.424,
     'L2_cond_Bm': 3.43}
    for name, (base, spread) in spreads.items():
        noise = np.random.default_rng([zlib.crc32(name.encode()), seed]).standard_normal(out[name].shape)
        drawn = base * np.exp(spread * noise) if base else spread * noise
        out[name] = jnp.asarray(drawn.astype(out[name].dtype))
    for name, factor in factors.items():
        out[name] = (out[name] * factor).astype(out[name].dtype)
    return out
```

```python
from contextlib import ExitStack

import concourse.bass as bass
from concourse import mybir

P = 128
F32 = mybir.dt.float32
I32 = mybir.dt.int32
U32 = mybir.dt.uint32
ALU = mybir.AluOpType
ACT = mybir.ActivationFunctionType

B, C, D = 32, 32, 256
KT = D // P
ROWS = B * C
BG = P // C
G = B // BG
NE1, NE2, NE3, RANK = 4, 8, 16, 16
R1, R2 = NE1 * RANK, NE2 * RANK
CH = 2
CW = ROWS // CH
BC = B // CH
LOADS3 = 4
EL = NE3 // LOADS3
IDS = 8


def cond_resid_kernel(nc, xT, wt, wpT, wb, b2p2, ab, q2, scales, consts, ids, w0, w3, b3, out):
    with ExitStack() as ctx:
        def sb(name, shape, dt=F32):
            return ctx.enter_context(nc.sbuf_tensor(name, shape, dt))

        def sem(name):
            return ctx.enter_context(nc.semaphore(name))

        xT_sb = sb("xT_sb", [P, KT, ROWS])
        wt_sb = sb("wt_sb", [P, KT, D])
        wpT_sb = sb("wpT_sb", [P, KT, D])
        b1T_sb = sb("b1T_sb", [P, KT, D])
        b2p2_sb = sb("b2p2_sb", [P, KT, D + R2])
        ab_sb = sb("ab_sb", [P, KT, 2 * R1])
        q2_sb = sb("q2_sb", [P, D])
        scales_sb = sb("scales_sb", [P, 2])
        consts_sb = sb("consts_sb", [P, 2])
        ids_sb = sb("ids_sb", [P, 3 * B + 2 * G], I32)
        ident = sb("ident", [P, P])
        row0 = sb("row0", [P, G], I32)
        expert = sb("expert", [P, B], I32)
        w0_rows = sb("w0_rows", [P, G, C])
        w0_bd = sb("w0_bd", [P, G, BG, C])
        bias = sb("bias", [P, G, D])
        mask1 = sb("mask1", [P, B])
        mask2 = sb("mask2", [P, B])
        p1 = sb("p1", [P, KT, R1])
        q1T = sb("q1T", [P, KT, R1])
        bp = sb("bp", [P, KT, D + R2])
        qb = sb("qb", [P, D + R2])
        z1 = sb("z1", [P, ROWS])
        z2 = sb("z2", [P, ROWS])
        y_sb = sb("y_sb", [P, G, D])
        x2T = sb("x2T", [P, G, KT, P])
        w3_sb = sb("w3_sb", [P, NE3, KT, D])
        w3_of = sb("w3_of", [P, B, KT, D])
        out_sb = sb("out_sb", [P, G, D])

        banks = [ctx.enter_context(nc.psum_tensor(f"bank{n}", [P, 512], F32)) for n in range(8)]
        p1_ps, q1T_ps = (banks[n][:, 0:KT * 2 * R1].rearrange("p (k r) -> p k r", k=KT) for n in (0, 7))
        bp_ps = [banks[1], banks[2]]
        qb_ps = banks[3]
        z1_ps = banks[4]
        z2_ps = [banks[5], banks[6]]
        y_ps = [banks[0], banks[1]]
        mix_ps = [banks[2], banks[3]]
        out_ps = [banks[4], banks[7]]

        load = {n: sem(f"load_{n}") for n in
                ("ids", "small", "ab", "wt", "wpT", "wb", "b2p2", "x0", "x1", "q2", "bias")}
        load_w0 = sem("load_w0")
        load_w3 = [sem(f"load_w3_{n}") for n in range(LOADS3)]
        stored = sem("stored")
        ident_zeroed = sem("ident_zeroed")
        zeroed = sem("zeroed")
        ident_ready = sem("ident_ready")
        rows_ready = sem("rows_ready")
        expert_ready = sem("expert_ready")
        b_ready = sem("b_ready")
        masks_ready = sem("masks_ready")
        w0_ready = sem("w0_ready")
        p1_done = sem("p1_done")
        q1_done = sem("q1_done")
        bp_done = sem("bp_done")
        qb_done = sem("qb_done")
        p1_ready = sem("p1_ready")
        q1_ready = sem("q1_ready")
        bp_ready = sem("bp_ready")
        qb_ready = sem("qb_ready")
        z1_done = sem("z1_done")
        z1_ready = sem("z1_ready")
        z2_done = sem("z2_done")
        z2_ready = sem("z2_ready")
        y_done = sem("y_done")
        y_ready = sem("y_ready")
        mix_done = sem("mix_done")
        mix_ready = sem("mix_ready")
        w3_ready = sem("w3_ready")
        w3_copied = sem("w3_copied")
        out_done = sem("out_done")
        out_ready = sem("out_ready")

        id_of_col = {1: ids_sb[:, 0:B], 2: ids_sb[:, B:2 * B], 3: ids_sb[:, 2 * B:3 * B]}
        id0_of_row = ids_sb[:, 3 * B:3 * B + G]
        id3_of_row = ids_sb[:, 3 * B + G:3 * B + 2 * G]
        rows = lambda g: slice(g * P, (g + 1) * P)
        tile = lambda k: slice(k * P, (k + 1) * P)
        chunk = lambda c: slice(c * CW, (c + 1) * CW)

        block = ctx.enter_context(nc.Block())

        @block.sync
        def _(sp):
            sp.dma_start(ids_sb[:, :], ids).then_inc(load["ids"], 16)
            sp.dma_start(ab_sb[:, :, :], ab).then_inc(load["ab"], 16)
            sp.dma_start(wt_sb[:, :, :], wt).then_inc(load["wt"], 16)
            sp.dma_start(b1T_sb[:, :, :], wb).then_inc(load["wb"], 16)
            sp.dma_start(xT_sb[:, :, chunk(0)], xT[:, :, chunk(0)]).then_inc(load["x0"], 16)
            sp.dma_start(xT_sb[:, :, chunk(1)], xT[:, :, chunk(1)]).then_inc(load["x1"], 16)
            for n in range(LOADS3):
                e = slice(n * EL, (n + 1) * EL)
                sp.dma_start(w3_sb[:, e, :, :], w3[:, e, :, :]).then_inc(load_w3[n], 16)
            for g in range(G):
                sp.wait_ge(out_ready, g + 1)
                sp.dma_start(out[rows(g), :], out_sb[:, g, :]).then_inc(stored, 16)
            sp.wait_ge(stored, 16 * G)

        @block.gpsimd
        def _(pool):
            nc.gpsimd.memset(ident[:, :], 0.0).then_inc(ident_zeroed, 1)
            pool.wait_ge(ident_zeroed, 1)
            nc.gpsimd.affine_select(out=ident[:, :], in_=ident[:, :], compare_op=ALU.not_equal, fill=1.0,
                                    base=0, pattern=[[-1, P]], channel_multiplier=1).then_inc(ident_ready, 1)
            pool.wait_ge(rows_ready, 1)
            for g in range(G):
                nc.gpsimd.indirect_dma_start(
                    out=w0_rows[:, g, :], out_offset=None, in_=w0[:, :],
                    in_offset=bass.IndirectOffsetOnAxis(ap=row0[:, g:g + 1].bitcast(U32), axis=0)
                ).then_inc(load_w0, 16)
            for g in range(G):
                nc.gpsimd.indirect_dma_start(
                    out=bias[:, g, :], out_offset=None, in_=b3[:, :],
                    in_offset=bass.IndirectOffsetOnAxis(ap=id3_of_row[:, g:g + 1].bitcast(U32), axis=0)
                ).then_inc(load["bias"], 16)
            pool.wait_ge(ident_ready, 1)
            for n in range(LOADS3):
                pool.wait_ge(load_w3[n], 16)
                for e in range(n * EL, (n + 1) * EL):
                    diag = w3_sb[:, e, :, :].rearrange("p k (t c) -> p (k t) c", c=P)[:, 0:4:3, :]
                    nc.gpsimd.tensor_tensor(diag, diag, ident[:, :].unsqueeze(1).to_broadcast([P, KT, P]),
                                            ALU.add).then_inc(w3_ready, 1)

        @block.scalar
        def _(act):
            act.dma_start(scales_sb[:, :], scales).then_inc(load["small"], 16)
            act.dma_start(consts_sb[:, :], consts).then_inc(load["small"], 16)
            act.dma_start(wpT_sb[:, :, :], wpT).then_inc(load["wpT"], 16)
            act.dma_start(b2p2_sb[:, :, :], b2p2).then_inc(load["b2p2"], 16)
            act.dma_start(q2_sb[:, :], q2).then_inc(load["q2"], 16)
            act.wait_ge(p1_done, 1)
            nc.scalar.copy(p1[:, :, :], p1_ps[:, :, 0:R1]).then_inc(p1_ready, 1)
            act.wait_ge(q1_done, 1)
            nc.scalar.copy(q1T[:, :, :], q1T_ps[:, :, R1:2 * R1]).then_inc(q1_ready, 1)
            for k in range(KT):
                act.wait_ge(bp_done, k + 1)
                nc.scalar.copy(bp[:, k, :], bp_ps[k][:, 0:D + R2]).then_inc(bp_ready, 1)
            act.wait_ge(qb_done, 1)
            nc.scalar.copy(qb[0:R1, :], qb_ps[0:R1, 0:D + R2]).then_inc(qb_ready, 1)
            for g in range(G + 1):
                if g < G:
                    act.wait_ge(y_done, g + 1)
                    nc.scalar.copy(y_sb[:, g, :], y_ps[g % 2][:, 0:D]).then_inc(y_ready, 1)
                if g > 0:
                    act.wait_ge(mix_done, g)
                    nc.scalar.copy(x2T[:, g - 1, :, :].rearrange("p k r -> p (k r)"),
                                   mix_ps[(g - 1) % 2][:, 0:D]).then_inc(mix_ready, 1)

        @block.vector
        def _(dve):
            nc.vector.memset(z1[R1:P, :], 0.0).then_inc(zeroed, 1)
            nc.vector.memset(qb[R1:P, :], 0.0).then_inc(zeroed, 1)
            nc.vector.memset(w0_bd[:, :, :, :], 0.0).then_inc(zeroed, 1)
            dve.wait_ge(load["ids"], 16)
            dve.wait_ge(load["small"], 32)
            nc.vector.tensor_scalar(row0[:, :], id0_of_row, float(C), consts_sb[:, 1:2],
                                    ALU.mult, ALU.add).then_inc(rows_ready, 1)
            nc.vector.tensor_scalar(expert[:, :], id_of_col[3], 0.0, float(NE3 - 1),
                                    ALU.max, ALU.min).then_inc(expert_ready, 1)
            nc.vector.tensor_scalar(mask1[:, :], id_of_col[1], consts_sb[:, 0:1], scales_sb[:, 0:1],
                                    ALU.is_equal, ALU.mult).then_inc(masks_ready, 1)
            nc.vector.tensor_scalar(mask2[:, :], id_of_col[2], consts_sb[:, 0:1], scales_sb[:, 1:2],
                                    ALU.is_equal, ALU.mult).then_inc(masks_ready, 1)
            dve.wait_ge(ident_ready, 1)
            two_idents = ident[:, :].unsqueeze(1).to_broadcast([P, KT, P])
            dve.wait_ge(load["wb"], 16)
            diag = b1T_sb[:, :, :].rearrange("p k (t c) -> p (k t) c", c=P)[:, 0:4:3, :]
            nc.vector.tensor_tensor(diag, diag, two_idents, ALU.add).then_inc(b_ready, 1)
            dve.wait_ge(load["b2p2"], 16)
            diag = b2p2_sb[:, :, :].rearrange("p k (t c) -> p (k t) c", c=P)[:, 0:5:4, :]
            nc.vector.tensor_tensor(diag, diag, two_idents, ALU.add).then_inc(b_ready, 1)
            dve.wait_ge(masks_ready, 2)
            dve.wait_ge(z1_done, 1)
            for c in range(CH):
                nc.vector.tensor_tensor(
                    z1[0:R1, chunk(c)].rearrange("p (b r) -> p b r", r=C),
                    z1_ps[c * R1:(c + 1) * R1, :].rearrange("p (b r) -> p b r", r=C),
                    mask1[0:R1, c * BC:(c + 1) * BC].unsqueeze(2).to_broadcast([R1, BC, C]),
                    ALU.mult).then_inc(z1_ready, 1)
            for c in range(CH):
                dve.wait_ge(z2_done, c + 1)
                nc.vector.tensor_tensor(
                    z2[:, chunk(c)].rearrange("p (b r) -> p b r", r=C),
                    z2_ps[c][:, :].rearrange("p (b r) -> p b r", r=C),
                    mask2[:, c * BC:(c + 1) * BC].unsqueeze(2).to_broadcast([P, BC, C]),
                    ALU.mult).then_inc(z2_ready, 1)
            dve.wait_ge(zeroed, 3)
            dve.wait_ge(load_w0, 16 * G)
            for q in range(BG):
                part = slice(q * C, (q + 1) * C)
                nc.vector.tensor_tensor(w0_bd[part, :, q, :], w0_rows[part, :, :],
                                        ident[part, part].unsqueeze(1).to_broadcast([C, G, C]),
                                        ALU.add).then_inc(w0_ready, 1)
            dve.wait_ge(expert_ready, 1)
            dve.wait_ge(w3_ready, NE3)
            for b0 in range(0, B, IDS):
                _, chosen = nc.values_load_multi_w_load_instructions(
                    expert[0:1, b0:b0 + IDS], engines=[nc.vector.engine], min_val=0, max_val=NE3 - 1,
                    skip_runtime_bounds_check_because="expert is brought into its range when it is made")
                for n, e in enumerate(chosen):
                    nc.vector.tensor_copy(w3_of[:, b0 + n, :, :].rearrange("p k d -> p (k d)"),
                                          w3_sb[:, bass.ds(e, 1), :, :].rearrange("p e k d -> p (e k d)")
                                          ).then_inc(w3_copied, 1)
            dve.wait_ge(load["bias"], 16 * G)
            for g in range(G):
                dve.wait_ge(out_done, g + 1)
                nc.vector.tensor_tensor(out_sb[:, g, :], out_ps[g % 2][:, 0:D], bias[:, g, :],
                                        ALU.add).then_inc(out_ready, 1)

        @block.tensor
        def _(pe):
            mm = nc.tensor.matmul

            pe.wait_ge(load["ab"], 16)
            pe.wait_ge(load["wt"], 16)
            for k in range(KT):
                for j in range(KT):
                    last = mm(p1_ps[:, k, :], wt_sb[:, j, tile(k)], ab_sb[:, j, :], start=j == 0, stop=j == KT - 1)
            last.then_inc(p1_done, 1)
            pe.wait_ge(load["wpT"], 16)
            for k in range(KT):
                for j in range(KT):
                    last = mm(q1T_ps[:, k, :], wpT_sb[:, j, tile(k)], ab_sb[:, j, :], start=j == 0, stop=j == KT - 1)
            last.then_inc(q1_done, 1)

            pe.wait_ge(b_ready, 2)
            for k in range(KT):
                for j in range(KT):
                    last = mm(bp_ps[k][:, 0:D + R2], b1T_sb[:, j, tile(k)], b2p2_sb[:, j, :],
                              start=j == 0, stop=j == KT - 1)
                last.then_inc(bp_done, 1)
            pe.wait_ge(q1_ready, 1)
            for j in range(KT):
                last = mm(qb_ps[0:R1, 0:D + R2], q1T[:, j, :], b2p2_sb[:, j, :], start=j == 0, stop=j == KT - 1)
            last.then_inc(qb_done, 1)

            pe.wait_ge(p1_ready, 1)
            pe.wait_ge(load["x0"], 16)
            pe.wait_ge(load["x1"], 16)
            for k in range(KT):
                for c in range(CH):
                    last = mm(z1_ps[c * R1:(c + 1) * R1, :], p1[:, k, :], xT_sb[:, k, chunk(c)],
                              start=k == 0, stop=k == KT - 1)
            last.then_inc(z1_done, 1)
            pe.wait_ge(bp_ready, KT)
            for c in range(CH):
                for k in range(KT):
                    mm(z2_ps[c][:, :], bp[:, k, D:D + R2], xT_sb[:, k, chunk(c)], start=k == 0, stop=False)
            pe.wait_ge(qb_ready, 1)
            pe.wait_ge(zeroed, 2)
            for c in range(CH):
                pe.wait_ge(z1_ready, c + 1)
                mm(z2_ps[c][:, :], qb[:, D:D + R2], z1[:, chunk(c)], start=False, stop=True).then_inc(z2_done, 1)

            def y_of(g):
                if g >= 2:
                    pe.wait_ge(y_ready, g - 1)
                y = y_ps[g % 2][:, 0:D]
                mm(y, xT_sb[:, 0, rows(g)], bp[:, 0, 0:D], start=True, stop=False)
                mm(y, xT_sb[:, 1, rows(g)], bp[:, 1, 0:D], start=False, stop=False)
                mm(y, z1[:, rows(g)], qb[:, 0:D], start=False, stop=False)
                pe.wait_ge(z2_ready, g // (G // CH) + 1)
                mm(y, z2[:, rows(g)], q2_sb[:, :], start=False, stop=True).then_inc(y_done, 1)

            def mix(g):
                pe.wait_ge(y_ready, g + 1)
                if g >= 2:
                    pe.wait_ge(mix_ready, g - 1)
                for k in range(KT):
                    last = mm(mix_ps[g % 2][:, tile(k)], y_sb[:, g, tile(k)],
                              w0_bd[:, g, :, :].rearrange("p q c -> p (q c)"), start=True, stop=True)
                last.then_inc(mix_done, 1)

            pe.wait_ge(load["q2"], 16)
            y_of(0)
            pe.wait_ge(w0_ready, BG)
            for g in range(1, G):
                y_of(g)
                mix(g - 1)
            mix(G - 1)

            for g in range(G):
                pe.wait_ge(mix_ready, g + 1)
                pe.wait_ge(w3_copied, (g + 1) * BG)
                if g >= 2:
                    pe.wait_ge(out_ready, g - 1)
                for k in range(KT):
                    for q in range(BG):
                        last = mm(out_ps[g % 2][q * C:(q + 1) * C, 0:D], x2T[:, g, k, q * C:(q + 1) * C],
                                  w3_of[:, g * BG + q, k, :], start=k == 0, stop=k == KT - 1)
                last.then_inc(out_done, 1)


def kernel(x, itok_B_1_198, itok_B_0_3, itok_B_0_6, itok_B_0_15, L0_cond_weights, L1_cond_W_base, L1_cond_Wt,
           L1_cond_A, L1_cond_B_w, L1_cond_Wp, L1_cond_scaling, L2_cond_W, L2_cond_A, L2_cond_Bm,
           L2_cond_scalings, L3_cond_W, L3_cond_b):
    import numpy as np
    import concourse.bacc as bacc
    from concourse.bass_utils import run_bass_kernel_spmd

    def tiled(a):
        return a.reshape(KT, P, -1).transpose(1, 0, 2)

    def by_group(ids):
        return np.repeat(ids.reshape(G, BG), C, axis=1).T

    x, w0, w3 = np.asarray(x), np.asarray(L0_cond_weights), np.asarray(L3_cond_W)
    id0, id1, id2, id3 = (np.asarray(a) for a in (itok_B_1_198, itok_B_0_3, itok_B_0_6, itok_B_0_15))
    ids = np.concatenate([np.broadcast_to(np.concatenate([id1, id2, id3]), (P, 3 * B)),
                          by_group(id0), by_group(id3)], axis=1)
    scales = np.stack([np.tile(np.repeat(np.asarray(L1_cond_scaling), RANK), P // R1),
                       np.repeat(np.asarray(L2_cond_scalings), RANK)], axis=1)
    consts = np.stack([np.arange(P) // RANK, np.arange(P) % C], axis=1).astype(np.float32)
    a1T = np.asarray(L1_cond_A).reshape(R1, D).T
    bwT = np.asarray(L1_cond_B_w).transpose(1, 0, 2).reshape(D, R1)
    p2 = np.asarray(L2_cond_A).reshape(R2, D).T
    feeds = {
        "xT": tiled(x.reshape(ROWS, D).T),
        "wt": tiled(np.asarray(L1_cond_Wt)),
        "wpT": tiled(np.asarray(L1_cond_Wp).T),
        "wb": tiled(np.asarray(L1_cond_W_base)),
        "b2p2": tiled(np.concatenate([np.asarray(L2_cond_W).T, p2], axis=1)),
        "ab": tiled(np.concatenate([a1T, bwT], axis=1)),
        "q2": np.asarray(L2_cond_Bm).transpose(0, 2, 1).reshape(R2, D),
        "scales": scales,
        "consts": consts,
        "ids": ids,
        "w0": w0.reshape(-1, C),
        "w3": w3.reshape(NE3, KT, P, D).transpose(2, 0, 1, 3),
        "b3": np.asarray(L3_cond_b),
    }
    feeds = {n: np.ascontiguousarray(a) for n, a in feeds.items()}
    nc = bacc.Bacc("TRN2", target_bir_lowering=False, num_devices=1)
    args = [nc.dram_tensor(n, a.shape, mybir.dt.from_np(a.dtype), kind="ExternalInput").ap()
            for n, a in feeds.items()]
    out = nc.dram_tensor("out", (ROWS, D), F32, kind="ExternalOutput").ap()
    cond_resid_kernel(nc, *args, out)
    got = run_bass_kernel_spmd(nc, [feeds], core_ids=[0]).results[0]["out"]
    return got.reshape(B, C, D)
```

```python
from contextlib import ExitStack

import concourse.bass as bass
from concourse import mybir

P = 128
F32 = mybir.dt.float32
I32 = mybir.dt.int32
U32 = mybir.dt.uint32
ALU = mybir.AluOpType
ACT = mybir.ActivationFunctionType

B, C, D = 32, 32, 256
KT = D // P
ROWS = B * C
BG = P // C
G = B // BG
NE1, NE2, NE3, RANK = 4, 8, 16, 16
R1, R2 = NE1 * RANK, NE2 * RANK
RG = BG * RANK
H = P // 2
PAIRS = G // 2
N0 = 200
LOADS3 = 8
EL = NE3 // LOADS3
EARLY0 = 4
WARM_UP = 3
AHEAD3 = 5
G3_DVE = 6


def cond_resid_kernel(nc, xT, wt, wpT, wb, b2p2, ab, q2, small, ids, w0, w3, b3, out):
    with ExitStack() as ctx:
        def sb(name, shape, dt=F32):
            return ctx.enter_context(nc.sbuf_tensor(name, shape, dt))

        def sem(name):
            return ctx.enter_context(nc.semaphore(name))

        xT_sb = sb("xT_sb", [P, KT, ROWS])
        wt_sb = sb("wt_sb", [P, KT, D])
        wpT_sb = sb("wpT_sb", [P, KT, D])
        b1T_sb = sb("b1T_sb", [P, KT, D])
        b2p2_sb = sb("b2p2_sb", [P, KT, D + R2])
        ab_sb = sb("ab_sb", [P, KT, 2 * R1])
        small_sb = sb("small_sb", [P, 1 + NE2 + 2 + BG])
        ids_sb = sb("ids_sb", [P, 4 * B + PAIRS + G], I32)
        chosen = sb("chosen", [1, 3, B], I32)
        zeros = sb("zeros", [P, 2 * P])
        ident = sb("ident", [P, P])
        q2_row = sb("q2_row", [P, PAIRS], I32)
        q2_pair = sb("q2_pair", [P, PAIRS, D])
        w0_bd = sb("w0_bd", [P, G, BG, C])
        bias = sb("bias", [P, G, D])
        mask1 = sb("mask1", [P, PAIRS, 2, BG])
        p1 = sb("p1", [P, KT, R1])
        q1T = sb("q1T", [P, KT, R1])
        b12 = sb("b12", [P, KT, D])
        p2_all = sb("p2_all", [P, KT + 2, R2])
        p2_of = sb("p2_of", [P, G, KT + 1, RG])
        z = [sb("z_even", [P, PAIRS, P]), sb("z_odd", [P, PAIRS, P])]
        qq = [sb("qq_even", [P, PAIRS, D]), sb("qq_odd", [P, PAIRS, D])]
        y_sb = sb("y_sb", [P, G, D])
        x2T = sb("x2T", [P, G, KT, P])
        w3_sb = sb("w3_sb", [P, NE3, KT, D])
        w3_of = sb("w3_of", [P, B, KT, D])
        out_sb = sb("out_sb", [P, G, D])

        banks = [ctx.enter_context(nc.psum_tensor(f"bank{n}", [P, 512], F32)) for n in range(8)]
        p1_ps, q1T_ps = (banks[n][:, 0:KT * 2 * R1].rearrange("p (k r) -> p k r", k=KT) for n in (0, 7))
        bp_ps = [banks[1], banks[2]]
        qb_ps = banks[3]
        z1_ps = banks[4]
        z2_ps = [banks[5], banks[6]]
        y_ps = [banks[0], banks[1]]
        mix_ps = [banks[2], banks[3]]
        out_ps = [banks[4], banks[7], banks[5], banks[6]]

        load = {n: sem(f"load_{n}") for n in
                ("ids", "small", "ab", "wt", "wpT", "wb", "b2p2", "x0", "x1", "q2")}
        load_w0 = [sem(f"load_w0_{g}") for g in range(G)]
        load_bias = [sem(f"load_bias_{g}") for g in range(G)]
        load_w3 = [sem(f"load_w3_{n}") for n in range(LOADS3)]
        stored = sem("stored")
        ident_zeroed = sem("ident_zeroed")
        ident_ready = sem("ident_ready")
        zeros_ready = sem("zeros_ready")
        w0_zeroed = sem("w0_zeroed")
        z_zeroed = sem("z_zeroed")
        p2_zeroed = sem("p2_zeroed")
        rows_ready = sem("rows_ready")
        chosen_ready = sem("chosen_ready")
        b_ready = sem("b_ready")
        p2_scaled = sem("p2_scaled")
        mask_ready = sem("mask_ready")
        w0_ready = sem("w0_ready")
        p1_done = sem("p1_done")
        q1_done = sem("q1_done")
        bp_done = sem("bp_done")
        qb_done = sem("qb_done")
        p1_ready = sem("p1_ready")
        q1_ready = sem("q1_ready")
        b1p2_ready = sem("b1p2_ready")
        b12_ready = sem("b12_ready")
        q1p2_ready = sem("q1p2_ready")
        q1b2_ready = sem("q1b2_ready")
        q2_ready = sem("q2_ready")
        picked_even = sem("picked_even")
        picked_odd = sem("picked_odd")
        z1_done = sem("z1_done")
        z1_ready = sem("z1_ready")
        z2_done = sem("z2_done")
        z2_ready = sem("z2_ready")
        y_done = sem("y_done")
        y_ready = sem("y_ready")
        mix_done = sem("mix_done")
        mix_ready = sem("mix_ready")
        w3_ready = sem("w3_ready")
        w3_copied = sem("w3_copied")
        w3_copied_last = sem("w3_copied_last")
        out_done = sem("out_done")
        out_ready = sem("out_ready")

        id1 = ids_sb[:, B:2 * B]
        id2_of_row = ids_sb[:, 4 * B:4 * B + PAIRS]
        id3_of_row = ids_sb[:, 4 * B + PAIRS:4 * B + PAIRS + G]
        s1_of_row, s2_all = small_sb[:, 0:1], small_sb[:, 1:1 + NE2]
        block_of_row, rank_of_row = small_sb[:, 1 + NE2:2 + NE2], small_sb[:, 2 + NE2:3 + NE2]
        in_block = small_sb[:, 3 + NE2:3 + NE2 + BG]
        ID0, ID2, ID3 = range(3)
        EXPERTS = {ID0: N0, ID2: NE2, ID3: NE3}
        EVEN, ODD = 0, 1
        Z1 = {EVEN: slice(H, P), ODD: slice(0, H)}
        Z2 = {EVEN: slice(0, H), ODD: slice(H, P)}
        SLOTS = {EVEN: slice(0, KT + 1), ODD: slice(1, KT + 2)}
        B1P2 = {EVEN: (1, 2), ODD: (0, 1)}
        Q1P2 = {EVEN: 0, ODD: 2}
        rows = lambda g: slice(g * P, (g + 1) * P)
        tile = lambda k: slice(k * P, (k + 1) * P)

        def registers(engine, which, b0, n):
            return nc.values_load_multi_w_load_instructions(
                chosen[0:1, which, b0:b0 + n], engines=[engine.engine], min_val=0, max_val=EXPERTS[which] - 1,
                skip_runtime_bounds_check_because="chosen is brought into its range when it is made")[1]

        def pick_p2(copy, g, adapters):
            for q, f in enumerate(adapters):
                yield copy(p2_of[:, g, :, q * RANK:(q + 1) * RANK],
                           p2_all[:, SLOTS[g % 2], bass.ds(f * RANK, RANK)])

        def copy_experts(copy, g, experts):
            for q, e in enumerate(experts):
                yield copy(w3_of[:, g * BG + q, :, :].rearrange("p k d -> p (k d)"),
                           w3_sb[:, bass.ds(e, 1), :, :].rearrange("p e k d -> p (e k d)"))

        block = ctx.enter_context(nc.Block())

        @block.sync
        def _(sp):
            sp.dma_start(wt_sb[:, :, :], wt).then_inc(load["wt"], 16)
            sp.dma_start(b2p2_sb[:, :, :], b2p2).then_inc(load["b2p2"], 16)
            sp.dma_start(b1T_sb[:, :, :], wb).then_inc(load["wb"], 16)
            sp.dma_start(xT_sb[:, 1, :], xT[:, 1, :]).then_inc(load["x1"], 16)
            sp.wait_ge(chosen_ready, 3)
            sp.wait_ge(w0_zeroed, 1)
            for g in range(G):
                for n in range(2 * g, min(2 * g + 2, LOADS3)):
                    e = slice(n * EL, (n + 1) * EL)
                    sp.dma_start(w3_sb[:, e, :, :], w3[:, e, :, :]).then_inc(load_w3[n], 16)
                for q, m in enumerate(registers(sp, ID0, g * BG, BG)):
                    sp.dma_start(w0_bd[q * C:(q + 1) * C, g, q, :],
                                 w0[bass.ds(m, 1), :, :].rearrange("m c d -> (m c) d")).then_inc(load_w0[g], 16)
            for g in range(G):
                sp.wait_ge(out_ready, g + 1)
                sp.dma_start(out[rows(g), :], out_sb[:, g, :]).then_inc(stored, 16)
            sp.wait_ge(stored, 16 * G)

        @block.gpsimd
        def _(pool):
            pool.dma_start(ids_sb[:, :], ids).then_inc(load["ids"], 16)
            pool.dma_start(small_sb[:, :], small).then_inc(load["small"], 16)
            nc.gpsimd.memset(ident[:, :], 0.0).then_inc(ident_zeroed, 1)
            pool.wait_ge(ident_zeroed, 1)
            nc.gpsimd.affine_select(out=ident[:, :], in_=ident[:, :], compare_op=ALU.not_equal, fill=1.0,
                                    base=0, pattern=[[-1, P]], channel_multiplier=1).then_inc(ident_ready, 1)
            pool.wait_ge(rows_ready, 1)
            for j in range(PAIRS):
                nc.gpsimd.indirect_dma_start(
                    out=q2_pair[:, j, :], out_offset=None, in_=q2[:, :],
                    in_offset=bass.IndirectOffsetOnAxis(ap=q2_row[:, j:j + 1].bitcast(U32), axis=0)
                ).then_inc(load["q2"], 16)
            pool.wait_ge(ident_ready, 1)
            for n in range(LOADS3):
                pool.wait_ge(load_w3[n], 16)
                for e in range(n * EL, (n + 1) * EL):
                    diag = w3_sb[:, e, :, :].rearrange("p k (t c) -> p (k t) c", c=P)[:, 0:4:3, :]
                    nc.gpsimd.tensor_tensor(diag, diag, ident[:, :].unsqueeze(1).to_broadcast([P, KT, P]),
                                            ALU.add).then_inc(w3_ready, 1)
            for g in range(G):
                nc.gpsimd.indirect_dma_start(
                    out=bias[:, g, :], out_offset=None, in_=b3[:, :],
                    in_offset=bass.IndirectOffsetOnAxis(ap=id3_of_row[:, g:g + 1].bitcast(U32), axis=0)
                ).then_inc(load_bias[g], 16)

        @block.scalar
        def _(act):
            act.dma_start(ab_sb[:, :, :], ab).then_inc(load["ab"], 16)
            act.dma_start(wpT_sb[:, :, :], wpT).then_inc(load["wpT"], 16)
            act.dma_start(xT_sb[:, 0, :], xT[:, 0, :]).then_inc(load["x0"], 16)
            act.wait_ge(p1_done, 1)
            nc.scalar.copy(p1[:, :, :], p1_ps[:, :, 0:R1]).then_inc(p1_ready, 1)
            act.wait_ge(q1_done, 1)
            nc.scalar.copy(q1T[:, :, :], q1T_ps[:, :, R1:2 * R1]).then_inc(q1_ready, 1)
            act.wait_ge(chosen_ready, 3)
            adapters = {j: registers(act, ID2, 2 * j * BG, BG) for j in range(PAIRS)}
            act.wait_ge(qb_done, 1)
            nc.scalar.copy(p2_all[H:P, 0, :], qb_ps[H:P, D:D + R2]).then_inc(q1p2_ready, 1)
            nc.scalar.copy(p2_all[0:H, KT + 1, :], qb_ps[0:H, D:D + R2]).then_inc(q1p2_ready, 1)
            act.wait_ge(b1p2_ready, KT)
            act.wait_ge(q1p2_ready, 2)
            act.wait_ge(p2_zeroed, 2)
            for j in range(PAIRS):
                for copied in pick_p2(nc.scalar.copy, 2 * j, adapters[j]):
                    copied.then_inc(picked_even, 1)
            for par in (EVEN, ODD):
                nc.scalar.copy(qq[par][Z1[par], :, :],
                               qb_ps[Z1[par], 0:D].unsqueeze(1).to_broadcast([H, PAIRS, D])).then_inc(q1b2_ready, 1)
            for g in range(G + 1):
                if g < G:
                    act.wait_ge(y_done, g + 1)
                    nc.scalar.copy(y_sb[:, g, :], y_ps[g % 2][:, 0:D]).then_inc(y_ready, 1)
                if g > 0:
                    act.wait_ge(mix_done, g)
                    nc.scalar.copy(x2T[:, g - 1, :, :].rearrange("p k r -> p (k r)"),
                                   mix_ps[(g - 1) % 2][:, 0:D]).then_inc(mix_ready, 1)

            act.wait_ge(w3_ready, NE3)
            for g in range(G3_DVE, G):
                for copied in copy_experts(nc.scalar.copy, g, registers(act, ID3, g * BG, BG)):
                    copied.then_inc(w3_copied_last, 1)

        @block.vector
        def _(dve):
            nc.vector.memset(zeros[:, :], 0.0).then_inc(zeros_ready, 1)
            nc.vector.memset(w0_bd[:, :, :, :], 0.0).then_inc(w0_zeroed, 1)
            nc.vector.memset(p2_all[0:H, 0, :], 0.0).then_inc(p2_zeroed, 1)
            nc.vector.memset(p2_all[H:P, KT + 1, :], 0.0).then_inc(p2_zeroed, 1)
            for par in (EVEN, ODD):
                nc.vector.memset(z[par][Z2[par], :, :], 0.0).then_inc(z_zeroed, 1)
            dve.wait_ge(load["ids"], 16)
            for which, first in ((ID0, 0), (ID2, 2 * B), (ID3, 3 * B)):
                nc.vector.tensor_scalar(chosen[:, which, :], ids_sb[0:1, first:first + B], 0.0,
                                        float(EXPERTS[which] - 1), ALU.max, ALU.min).then_inc(chosen_ready, 1)
            dve.wait_ge(load["small"], 16)
            nc.vector.tensor_scalar(q2_row[:, :], id2_of_row, float(RANK), rank_of_row,
                                    ALU.mult, ALU.add).then_inc(rows_ready, 1)
            nc.vector.tensor_scalar(mask1[:, :, :, :].rearrange("p j e q -> p (j e q)"), id1, block_of_row,
                                    s1_of_row, ALU.is_equal, ALU.mult).then_inc(mask_ready, 1)
            dve.wait_ge(ident_ready, 1)
            two_idents = ident[:, :].unsqueeze(1).to_broadcast([P, KT, P])
            dve.wait_ge(load["b2p2"], 16)
            diag = b2p2_sb[:, :, :].rearrange("p k (t c) -> p (k t) c", c=P)[:, 0:5:4, :]
            nc.vector.tensor_tensor(diag, diag, two_idents, ALU.add).then_inc(b_ready, 1)
            for k in range(KT):
                p2 = b2p2_sb[:, k, D:D + R2].rearrange("p (f r) -> p f r", r=RANK)
                nc.vector.tensor_tensor(p2, p2, s2_all.unsqueeze(2).to_broadcast([P, NE2, RANK]),
                                        ALU.mult).then_inc(p2_scaled, 1)
            dve.wait_ge(load["wb"], 16)
            diag = b1T_sb[:, :, :].rearrange("p k (t c) -> p (k t) c", c=P)[:, 0:4:3, :]
            nc.vector.tensor_tensor(diag, diag, two_idents, ALU.add).then_inc(b_ready, 1)
            dve.wait_ge(chosen_ready, 3)
            adapters = {j: registers(dve, ID2, (2 * j + 1) * BG, BG) for j in range(PAIRS)}
            for k in range(KT):
                dve.wait_ge(bp_done, k + 1)
                nc.vector.tensor_copy(p2_all[:, 1 + k, :], bp_ps[k][:, D:D + R2]).then_inc(b1p2_ready, 1)
            for k in range(KT):
                nc.vector.tensor_copy(b12[:, k, :], bp_ps[k][:, 0:D]).then_inc(b12_ready, 1)
            dve.wait_ge(b1p2_ready, KT)
            dve.wait_ge(q1p2_ready, 2)
            dve.wait_ge(p2_zeroed, 2)
            dve.wait_ge(mask_ready, 1)
            for j in range(PAIRS):
                for copied in pick_p2(nc.vector.tensor_copy, 2 * j + 1, adapters[j]):
                    copied.then_inc(picked_odd, 1)
                if j == 1:
                    dve.wait_ge(z1_done, 1)
                    for par in (EVEN, ODD):
                        nc.vector.tensor_tensor(
                            z[par][Z1[par], :, :].rearrange("p j (q c) -> p j q c", q=BG),
                            z1_ps[Z1[par], :].rearrange("p (j q c) -> p j q c", j=PAIRS, q=BG),
                            mask1[Z1[par], :, par, :].unsqueeze(3).to_broadcast([H, PAIRS, BG, C]),
                            ALU.mult).then_inc(z1_ready, 1)
            dve.wait_ge(load["q2"], 16 * PAIRS)
            for par in (EVEN, ODD):
                nc.vector.tensor_copy(qq[par][Z2[par], :, :], q2_pair[Z2[par], :, :]).then_inc(q2_ready, 1)
            dve.wait_ge(z_zeroed, 2)
            def layer0_residual(g):
                dve.wait_ge(load_w0[g], 16 * BG)
                whole = w0_bd[:, g, :, :].rearrange("p q c -> p (q c)")
                nc.vector.tensor_tensor(whole, whole, ident[:, :], ALU.add).then_inc(w0_ready, 1)

            for n in range(2):
                dve.wait_ge(z2_done, n + 1)
                for par in (EVEN, ODD):
                    nc.vector.tensor_tensor(
                        z[par][Z2[par], 2 * n:2 * n + 2, :].rearrange("p j (q c) -> p j q c", q=BG),
                        z2_ps[n][Z2[par], 0:2 * P].rearrange("p (j q c) -> p j q c", j=2, q=BG),
                        in_block[Z2[par], :].unsqueeze(1).unsqueeze(3).to_broadcast([H, 2, BG, C]),
                        ALU.mult).then_inc(z2_ready, 1)
                if n == 0:
                    for g in range(EARLY0):
                        layer0_residual(g)

            dve.wait_ge(w3_ready, NE3)
            for g in range(AHEAD3):
                for copied in copy_experts(nc.vector.tensor_copy, g, registers(dve, ID3, g * BG, BG)):
                    copied.then_inc(w3_copied, 1)
                if EARLY0 + g < G:
                    layer0_residual(EARLY0 + g)
            for g in range(G):
                if AHEAD3 + g < G3_DVE:
                    ahead = AHEAD3 + g
                    for copied in copy_experts(nc.vector.tensor_copy, ahead, registers(dve, ID3, ahead * BG, BG)):
                        copied.then_inc(w3_copied, 1)
                dve.wait_ge(load_bias[g], 16)
                dve.wait_ge(out_done, g + 1)
                nc.vector.tensor_tensor(out_sb[:, g, :], out_ps[g % len(out_ps)][:, 0:D], bias[:, g, :],
                                        ALU.add).then_inc(out_ready, 1)

        @block.tensor
        def _(pe):
            mm = nc.tensor.matmul

            pe.wait_ge(zeros_ready, 1)
            for _ in range(WARM_UP):
                mm(z2_ps[0][:, 0:2 * P], zeros[:, 0:P], zeros[:, 0:2 * P], start=True, stop=True)

            pe.wait_ge(load["ab"], 16)
            pe.wait_ge(load["wt"], 16)
            for k in range(KT):
                for j in range(KT):
                    last = mm(p1_ps[:, k, :], wt_sb[:, j, tile(k)], ab_sb[:, j, :], start=j == 0, stop=j == KT - 1)
            last.then_inc(p1_done, 1)
            pe.wait_ge(load["wpT"], 16)
            for k in range(KT):
                for j in range(KT):
                    last = mm(q1T_ps[:, k, :], wpT_sb[:, j, tile(k)], ab_sb[:, j, :], start=j == 0, stop=j == KT - 1)
            last.then_inc(q1_done, 1)

            pe.wait_ge(b_ready, 2)
            pe.wait_ge(p2_scaled, KT)
            for k in range(KT):
                for j in range(KT):
                    last = mm(bp_ps[k][:, 0:D + R2], b1T_sb[:, j, tile(k)], b2p2_sb[:, j, :],
                              start=j == 0, stop=j == KT - 1)
                last.then_inc(bp_done, 1)
            pe.wait_ge(q1_ready, 1)
            for j in range(KT):
                for half in (slice(0, H), slice(H, P)):
                    last = mm(qb_ps[half, 0:D + R2], q1T[:, j, :], b2p2_sb[:, j, :], start=j == 0, stop=j == KT - 1)
            last.then_inc(qb_done, 1)

            pe.wait_ge(p1_ready, 1)
            pe.wait_ge(load["x0"], 16)
            pe.wait_ge(load["x1"], 16)
            for k in range(KT):
                xT_pairs = xT_sb[:, k, :].rearrange("p (j e r) -> p j e r", j=PAIRS, e=2)
                for par in (EVEN, ODD):
                    last = mm(z1_ps[Z1[par], :].rearrange("p (j r) -> p j r", j=PAIRS), p1[:, k, :],
                              xT_pairs[:, :, par, :], start=k == 0, stop=k == KT - 1)
            last.then_inc(z1_done, 1)

            def y_from_x(g):
                if g >= 2:
                    pe.wait_ge(y_ready, g - 1)
                for k in range(KT):
                    mm(y_ps[g % 2][:, 0:D], xT_sb[:, k, rows(g)], b12[:, k, :], start=k == 0, stop=False)

            def y_from_z(g):
                j, par = divmod(g, 2)
                pe.wait_ge(z2_ready, 2 * (j // 2) + par + 1)
                mm(y_ps[g % 2][:, 0:D], z[par][:, j, :], qq[par][:, j, :], start=False, stop=True).then_inc(y_done, 1)

            def z2_of(j):
                pe.wait_ge(picked_even, BG * (j + 1))
                pe.wait_ge(picked_odd, BG * (j + 1))
                ps = {par: z2_ps[j // 2][Z2[par], (j % 2) * P:(j % 2 + 1) * P] for par in (EVEN, ODD)}
                for k in range(KT):
                    for par in (EVEN, ODD):
                        mm(ps[par], p2_of[:, 2 * j + par, B1P2[par][k], :], xT_sb[:, k, rows(2 * j + par)],
                           start=k == 0, stop=False)
                pe.wait_ge(z1_ready, 2)
                pe.wait_ge(z_zeroed, 2)
                for par in (EVEN, ODD):
                    last = mm(ps[par], p2_of[:, 2 * j + par, Q1P2[par], :], z[par][:, j, :], start=False, stop=True)
                return last

            def mix(g):
                pe.wait_ge(y_ready, g + 1)
                pe.wait_ge(w0_ready, g + 1)
                if g >= 2:
                    pe.wait_ge(mix_ready, g - 1)
                for k in range(KT):
                    last = mm(mix_ps[g % 2][:, tile(k)], y_sb[:, g, tile(k)],
                              w0_bd[:, g, :, :].rearrange("p q c -> p (q c)"), start=True, stop=True)
                last.then_inc(mix_done, 1)

            pe.wait_ge(b12_ready, KT)
            y_from_x(0)
            y_from_x(1)
            for j in range(PAIRS):
                last = z2_of(j)
                if j % 2:
                    last.then_inc(z2_done, 1)
            pe.wait_ge(q2_ready, 2)
            pe.wait_ge(q1b2_ready, 2)
            y_from_z(0)
            y_from_z(1)
            for g in range(2, G):
                mix(g - 2)
                y_from_x(g)
                y_from_z(g)
            mix(G - 2)
            mix(G - 1)

            for g in range(G):
                pe.wait_ge(mix_ready, g + 1)
                if g < G3_DVE:
                    pe.wait_ge(w3_copied, (g + 1) * BG)
                else:
                    pe.wait_ge(w3_copied_last, (g + 1 - G3_DVE) * BG)
                if g >= len(out_ps):
                    pe.wait_ge(out_ready, g + 1 - len(out_ps))
                for k in range(KT):
                    for q in range(BG):
                        last = mm(out_ps[g % len(out_ps)][q * C:(q + 1) * C, 0:D], x2T[:, g, k, q * C:(q + 1) * C],
                                  w3_of[:, g * BG + q, k, :], start=k == 0, stop=k == KT - 1)
                last.then_inc(out_done, 1)


def kernel(x, itok_B_1_198, itok_B_0_3, itok_B_0_6, itok_B_0_15, L0_cond_weights, L1_cond_W_base, L1_cond_Wt,
           L1_cond_A, L1_cond_B_w, L1_cond_Wp, L1_cond_scaling, L2_cond_W, L2_cond_A, L2_cond_Bm,
           L2_cond_scalings, L3_cond_W, L3_cond_b):
    import numpy as np
    import concourse.bacc as bacc
    from concourse.bass_utils import run_bass_kernel_spmd

    def tiled(a):
        return a.reshape(KT, P, -1).transpose(1, 0, 2)

    def by_group(ids):
        return np.repeat(ids.reshape(G, BG), C, axis=1).T

    x, w0, w3 = np.asarray(x), np.asarray(L0_cond_weights), np.asarray(L3_cond_W)
    id0, id1, id2, id3 = (np.asarray(a) for a in (itok_B_1_198, itok_B_0_3, itok_B_0_6, itok_B_0_15))
    id2_of_row = np.repeat(id2.reshape(PAIRS, 2 * BG), RANK, axis=1).T
    ids = np.concatenate([np.broadcast_to(np.concatenate([id0, id1, id2, id3]), (P, 4 * B)),
                          id2_of_row, by_group(id3)], axis=1)
    s1, s2 = np.asarray(L1_cond_scaling), np.asarray(L2_cond_scalings)
    s1_s2 = np.concatenate([np.tile(np.repeat(s1, RANK), P // R1)[:, None], np.broadcast_to(s2, (P, NE2))], axis=1)
    p = np.arange(P)[:, None]
    blocks = np.concatenate([p % H // RANK, p % RANK, p % H // RANK == np.arange(BG)], axis=1).astype(np.float32)
    a1T = np.asarray(L1_cond_A).reshape(R1, D).T
    bwT = np.asarray(L1_cond_B_w).transpose(1, 0, 2).reshape(D, R1)
    p2 = np.asarray(L2_cond_A).reshape(R2, D).T
    feeds = {
        "xT": tiled(x.reshape(ROWS, D).T),
        "wt": tiled(np.asarray(L1_cond_Wt)),
        "wpT": tiled(np.asarray(L1_cond_Wp).T),
        "wb": tiled(np.asarray(L1_cond_W_base)),
        "b2p2": tiled(np.concatenate([np.asarray(L2_cond_W).T, p2], axis=1)),
        "ab": tiled(np.concatenate([a1T, bwT], axis=1)),
        "q2": np.asarray(L2_cond_Bm).transpose(0, 2, 1).reshape(R2, D),
        "small": np.concatenate([s1_s2, blocks], axis=1),
        "ids": ids,
        "w0": w0,
        "w3": w3.reshape(NE3, KT, P, D).transpose(2, 0, 1, 3),
        "b3": np.asarray(L3_cond_b),
    }
    feeds = {n: np.ascontiguousarray(a) for n, a in feeds.items()}
    nc = bacc.Bacc("TRN2", target_bir_lowering=False, num_devices=1)
    args = [nc.dram_tensor(n, a.shape, mybir.dt.from_np(a.dtype), kind="ExternalInput").ap()
            for n, a in feeds.items()]
    out = nc.dram_tensor("out", (ROWS, D), F32, kind="ExternalOutput").ap()
    cond_resid_kernel(nc, *args, out)
    got = run_bass_kernel_spmd(nc, [feeds], core_ids=[0]).results[0]["out"]
    return got.reshape(B, C, D)
```

```python
from contextlib import ExitStack

import concourse.bass as bass
from concourse import mybir

P = 128
F32 = mybir.dt.float32
F32R = mybir.dt.float32r
I32 = mybir.dt.int32
U32 = mybir.dt.uint32
ALU = mybir.AluOpType

B, C, D = 32, 32, 256
KT = D // P
ROWS = B * C
BG = P // C
G = B // BG
NE1, NE2, NE3, RANK = 4, 8, 16, 16
R1, R2 = NE1 * RANK, NE2 * RANK
RG = BG * RANK
H = P // 2
PAIRS = G // 2
N0 = 200
LOADS3 = 8
LOADS3_POOL = 7
EL = NE3 // LOADS3
EARLY0 = 2
BEFORE3 = 5
PICKED_BY_ACT = (0, 1, 2, 4, 6)
PICKED_BY_DVE = (3, 5, 7)
WARM_UP = 3
TURN3 = 4
W3_BEFORE_W0 = {0: (0, 1), 2: (2, 3), 3: (4, 5), 4: (6, 7)}
G3_DVE = 5


def cond_resid_kernel(nc, xT, wt_ab, wpT, wb, b2p2, q2, small, ids, w0, w3, b3, out):
    with ExitStack() as ctx:
        def sb(name, shape, dt=F32):
            return ctx.enter_context(nc.sbuf_tensor(name, shape, dt))

        def sem(name):
            return ctx.enter_context(nc.semaphore(name))

        xT_sb = sb("xT_sb", [P, KT, ROWS])
        wt_ab_sb = sb("wt_ab_sb", [P, KT, D + 2 * R1])
        wpT_sb = sb("wpT_sb", [P, KT, D])
        b1T_sb = sb("b1T_sb", [P, KT, D])
        b2p2_sb = sb("b2p2_sb", [P, KT, D + R2])
        small_sb = sb("small_sb", [P, 1 + NE2 + 2 + BG])
        ids_sb = sb("ids_sb", [P, 4 * B + PAIRS + G], I32)
        chosen = sb("chosen", [1, 3, B], I32)
        zeros = sb("zeros", [P, 2 * P])
        ident = sb("ident", [P, P])
        q2_row = sb("q2_row", [P, PAIRS], I32)
        q2_pair = sb("q2_pair", [P, PAIRS, D])
        w0_bd = sb("w0_bd", [P, G, BG, C])
        bias = sb("bias", [P, G, D])
        mask1 = sb("mask1", [P, PAIRS, 2, BG])
        p1 = sb("p1", [P, KT, R1])
        q1T = sb("q1T", [P, KT, R1])
        x_hi, x_lo = (sb(f"x_{part}", [P, KT, ROWS], F32R) for part in ("hi", "lo"))
        b12_hi, b12_lo = (sb(f"b12_{part}", [P, KT, D], F32R) for part in ("hi", "lo"))
        p2_all = sb("p2_all", [P, KT + 2, R2])
        p2_of = sb("p2_of", [P, G, KT + 1, RG])
        z = [sb("z_even", [P, PAIRS, P]), sb("z_odd", [P, PAIRS, P])]
        qq = [sb("qq_even", [P, PAIRS, D]), sb("qq_odd", [P, PAIRS, D])]
        y_sb = sb("y_sb", [P, G, D])
        x2T = sb("x2T", [P, G, KT, P])
        w3_sb = sb("w3_sb", [P, NE3, KT, D])
        w3_of = sb("w3_of", [P, B, KT, D])
        out_sb = sb("out_sb", [P, G, D])

        banks = [ctx.enter_context(nc.psum_tensor(f"bank{n}", [P, 512], F32)) for n in range(8)]
        p1_ps, q1T_ps = (banks[n][:, 0:KT * 2 * R1].rearrange("p (k r) -> p k r", k=KT) for n in (0, 7))
        bp_ps = [banks[1], banks[2]]
        qb_ps = banks[3]
        z1_ps = banks[4]
        z2_ps = [banks[5], banks[6]]
        y_ps = [banks[0], banks[1], banks[7]]
        mix_ps = [banks[2], banks[3]]
        out_ps = [banks[4], banks[5], banks[6]]

        load = {n: sem(f"load_{n}") for n in
                ("ids", "small", "wt_ab", "wpT", "wb", "b2p2", "x0", "x1", "q2")}
        load_w0 = [sem(f"load_w0_{g}") for g in range(G)]
        load_bias = [sem(f"load_bias_{g}") for g in range(G)]
        load_w3 = [sem(f"load_w3_{n}") for n in range(LOADS3)]
        stored = sem("stored")
        ident_zeroed = sem("ident_zeroed")
        ident_ready = sem("ident_ready")
        zeros_ready = sem("zeros_ready")
        w0_zeroed = sem("w0_zeroed")
        z_zeroed = sem("z_zeroed")
        p2_zeroed = sem("p2_zeroed")
        rows_ready = sem("rows_ready")
        chosen_ready = sem("chosen_ready")
        b_ready = sem("b_ready")
        p2_scaled = sem("p2_scaled")
        mask_ready = sem("mask_ready")
        w0_ready = sem("w0_ready")
        p1_done = sem("p1_done")
        q1_done = sem("q1_done")
        bp_done = sem("bp_done")
        qb_done = sem("qb_done")
        p1_ready = sem("p1_ready")
        q1_ready = sem("q1_ready")
        b1p2_ready = sem("b1p2_ready")
        x_hi_ready = sem("x_hi_ready")
        x_lo_ready = sem("x_lo_ready")
        b12_hi_ready = sem("b12_hi_ready")
        b12_lo_ready = sem("b12_lo_ready")
        q1p2_ready = sem("q1p2_ready")
        q1b2_ready = sem("q1b2_ready")
        q2_even_ready = sem("q2_even_ready")
        q2_odd_ready = sem("q2_odd_ready")
        picked = [sem(f"picked_{g}") for g in range(G)]
        z1_done = sem("z1_done")
        z1_ready = sem("z1_ready")
        z2_done = sem("z2_done")
        z2_ready = sem("z2_ready")
        y_done = sem("y_done")
        y_ready = sem("y_ready")
        mix_done = sem("mix_done")
        mix_ready = sem("mix_ready")
        w3_ready = sem("w3_ready")
        w3_last_ready = sem("w3_last_ready")
        w3_copied = sem("w3_copied")
        w3_copied_last = sem("w3_copied_last")
        out_done = sem("out_done")
        out_ready = sem("out_ready")

        id1 = ids_sb[:, B:2 * B]
        id2_of_row = ids_sb[:, 4 * B:4 * B + PAIRS]
        id3_of_row = ids_sb[:, 4 * B + PAIRS:4 * B + PAIRS + G]
        s1_of_row, s2_all = small_sb[:, 0:1], small_sb[:, 1:1 + NE2]
        block_of_row, rank_of_row = small_sb[:, 1 + NE2:2 + NE2], small_sb[:, 2 + NE2:3 + NE2]
        in_block = small_sb[:, 3 + NE2:3 + NE2 + BG]
        ID0, ID2, ID3 = range(3)
        EXPERTS = {ID0: N0, ID2: NE2, ID3: NE3}
        EVEN, ODD = 0, 1
        Z1 = {EVEN: slice(H, P), ODD: slice(0, H)}
        Z2 = {EVEN: slice(0, H), ODD: slice(H, P)}
        SLOTS = {EVEN: slice(0, KT + 1), ODD: slice(1, KT + 2)}
        B1P2 = {EVEN: (1, 2), ODD: (0, 1)}
        Q1P2 = {EVEN: 0, ODD: 2}
        rows = lambda g: slice(g * P, (g + 1) * P)
        tile = lambda k: slice(k * P, (k + 1) * P)

        def registers(engine, which, b0, n):
            return nc.values_load_multi_w_load_instructions(
                chosen[0:1, which, b0:b0 + n], engines=[engine.engine], min_val=0, max_val=EXPERTS[which] - 1,
                skip_runtime_bounds_check_because="chosen is brought into its range when it is made")[1]

        def pick_p2(copy, g, adapters):
            for q, f in enumerate(adapters):
                yield copy(p2_of[:, g, :, q * RANK:(q + 1) * RANK],
                           p2_all[:, SLOTS[g % 2], bass.ds(f * RANK, RANK)])

        def copy_experts(copy, g, experts):
            for q, e in enumerate(experts):
                yield copy(w3_of[:, g * BG + q, :, :].rearrange("p k d -> p (k d)"),
                           w3_sb[:, bass.ds(e, 1), :, :].rearrange("p e k d -> p (e k d)"))

        def layer3_residual(engine, e):
            diag = w3_sb[:, e, :, :].rearrange("p k (t c) -> p (k t) c", c=P)[:, 0:4:3, :]
            return engine.tensor_tensor(diag, diag, ident[:, :].unsqueeze(1).to_broadcast([P, KT, P]), ALU.add)

        block = ctx.enter_context(nc.Block())

        @block.sync
        def _(sp):
            sp.dma_start(wt_ab_sb[:, :, :], wt_ab).then_inc(load["wt_ab"], 16)
            sp.dma_start(wpT_sb[:, :, :], wpT).then_inc(load["wpT"], 16)
            sp.dma_start(b1T_sb[:, :, :], wb).then_inc(load["wb"], 16)
            sp.dma_start(xT_sb[:, 0, :], xT[:, 0, :]).then_inc(load["x0"], 16)
            sp.dma_start(xT_sb[:, 1, :], xT[:, 1, :]).then_inc(load["x1"], 16)
            sp.wait_ge(chosen_ready, 3)
            sp.wait_ge(w0_zeroed, 1)
            for j in range(PAIRS):
                matrices = registers(sp, ID0, 2 * j * BG, 2 * BG)
                for g in (2 * j, 2 * j + 1):
                    for n in W3_BEFORE_W0.get(g, ()):
                        e = slice(n * EL, (n + 1) * EL)
                        sp.dma_start(w3_sb[:, e, :, :], w3[:, e, :, :]).then_inc(load_w3[n], 16)
                    for q in range(BG):
                        sp.dma_start(w0_bd[q * C:(q + 1) * C, g, q, :],
                                     w0[bass.ds(matrices[g % 2 * BG + q], 1), :, :].rearrange("m c d -> (m c) d")
                                     ).then_inc(load_w0[g], 16)
            for g in range(G):
                sp.wait_ge(out_ready, g + 1)
                sp.dma_start(out[rows(g), :], out_sb[:, g, :]).then_inc(stored, 16)
            sp.wait_ge(stored, 16 * G)

        @block.gpsimd
        def _(pool):
            pool.dma_start(ids_sb[:, :], ids).then_inc(load["ids"], 16)
            nc.gpsimd.memset(ident[:, :], 0.0).then_inc(ident_zeroed, 1)
            pool.wait_ge(ident_zeroed, 1)
            nc.gpsimd.affine_select(out=ident[:, :], in_=ident[:, :], compare_op=ALU.not_equal, fill=1.0,
                                    base=0, pattern=[[-1, P]], channel_multiplier=1).then_inc(ident_ready, 1)
            pool.wait_ge(rows_ready, 1)
            for j in range(PAIRS):
                nc.gpsimd.indirect_dma_start(
                    out=q2_pair[:, j, :], out_offset=None, in_=q2[:, :],
                    in_offset=bass.IndirectOffsetOnAxis(ap=q2_row[:, j:j + 1].bitcast(U32), axis=0)
                ).then_inc(load["q2"], 16)
            pool.wait_ge(ident_ready, 1)
            for n in range(LOADS3_POOL):
                pool.wait_ge(load_w3[n], 16)
                for e in range(n * EL, (n + 1) * EL):
                    layer3_residual(nc.gpsimd, e).then_inc(w3_ready, 1)
            for g in range(G):
                nc.gpsimd.indirect_dma_start(
                    out=bias[:, g, :], out_offset=None, in_=b3[:, :],
                    in_offset=bass.IndirectOffsetOnAxis(ap=id3_of_row[:, g:g + 1].bitcast(U32), axis=0)
                ).then_inc(load_bias[g], 16)

        @block.scalar
        def _(act):
            act.dma_start(small_sb[:, :], small).then_inc(load["small"], 16)
            act.dma_start(b2p2_sb[:, :, :], b2p2).then_inc(load["b2p2"], 16)
            act.wait_ge(p1_done, 1)
            nc.scalar.copy(p1[:, :, :], p1_ps[:, :, 0:R1]).then_inc(p1_ready, 1)
            act.wait_ge(load["x0"], 16)
            nc.scalar.copy(x_hi[:, 0, :], xT_sb[:, 0, :]).then_inc(x_hi_ready, 1)
            act.wait_ge(q1_done, 1)
            nc.scalar.copy(q1T[:, :, :], q1T_ps[:, :, R1:2 * R1]).then_inc(q1_ready, 1)
            act.wait_ge(load["x1"], 16)
            nc.scalar.copy(x_hi[:, 1, :], xT_sb[:, 1, :]).then_inc(x_hi_ready, 1)
            act.wait_ge(chosen_ready, 3)
            adapters = {g: registers(act, ID2, g * BG, BG) for g in PICKED_BY_ACT}
            act.wait_ge(qb_done, 1)
            nc.scalar.copy(p2_all[H:P, 0, :], qb_ps[H:P, D:D + R2]).then_inc(q1p2_ready, 1)
            nc.scalar.copy(p2_all[0:H, KT + 1, :], qb_ps[0:H, D:D + R2]).then_inc(q1p2_ready, 1)
            act.wait_ge(b1p2_ready, KT)
            act.wait_ge(q1p2_ready, 2)
            act.wait_ge(p2_zeroed, 2)
            for g in PICKED_BY_ACT:
                for copied in pick_p2(nc.scalar.copy, g, adapters[g]):
                    copied.then_inc(picked[g], 1)
            for par in (EVEN, ODD):
                nc.scalar.copy(qq[par][Z1[par], :, :],
                               qb_ps[Z1[par], 0:D].unsqueeze(1).to_broadcast([H, PAIRS, D])).then_inc(q1b2_ready, 1)
            act.wait_ge(load["q2"], 16 * PAIRS)
            nc.scalar.copy(qq[ODD][Z2[ODD], :, :], q2_pair[Z2[ODD], :, :]).then_inc(q2_odd_ready, 1)
            def last_experts():
                act.wait_ge(w3_ready, LOADS3_POOL * EL)
                act.wait_ge(w3_last_ready, NE3 - LOADS3_POOL * EL)
                for g in range(G3_DVE, G):
                    yield from copy_experts(nc.scalar.copy, g, registers(act, ID3, g * BG, BG))

            copies = last_experts()
            for g in range(G + 1):
                if g < G:
                    act.wait_ge(y_done, g + 1)
                    nc.scalar.copy(y_sb[:, g, :], y_ps[g % len(y_ps)][:, 0:D]).then_inc(y_ready, 1)
                if g > 0:
                    act.wait_ge(mix_done, g)
                    nc.scalar.copy(x2T[:, g - 1, :, :].rearrange("p k r -> p (k r)"),
                                   mix_ps[(g - 1) % 2][:, 0:D]).then_inc(mix_ready, 1)
                if g >= TURN3:
                    next(copies).then_inc(w3_copied_last, 1)

            for copied in copies:
                copied.then_inc(w3_copied_last, 1)

        @block.vector
        def _(dve):
            nc.vector.memset(zeros[:, :], 0.0).then_inc(zeros_ready, 1)
            nc.vector.memset(w0_bd[:, :, :, :], 0.0).then_inc(w0_zeroed, 1)
            nc.vector.memset(p2_all[0:H, 0, :], 0.0).then_inc(p2_zeroed, 1)
            nc.vector.memset(p2_all[H:P, KT + 1, :], 0.0).then_inc(p2_zeroed, 1)
            for par in (EVEN, ODD):
                nc.vector.memset(z[par][Z2[par], :, :], 0.0).then_inc(z_zeroed, 1)
            dve.wait_ge(load["ids"], 16)
            for which, first in ((ID0, 0), (ID2, 2 * B), (ID3, 3 * B)):
                nc.vector.tensor_scalar(chosen[:, which, :], ids_sb[0:1, first:first + B], 0.0,
                                        float(EXPERTS[which] - 1), ALU.max, ALU.min).then_inc(chosen_ready, 1)
            dve.wait_ge(load["small"], 16)
            nc.vector.tensor_scalar(q2_row[:, :], id2_of_row, float(RANK), rank_of_row,
                                    ALU.mult, ALU.add).then_inc(rows_ready, 1)
            nc.vector.tensor_scalar(mask1[:, :, :, :].rearrange("p j e q -> p (j e q)"), id1, block_of_row,
                                    s1_of_row, ALU.is_equal, ALU.mult).then_inc(mask_ready, 1)
            dve.wait_ge(ident_ready, 1)
            two_idents = ident[:, :].unsqueeze(1).to_broadcast([P, KT, P])
            dve.wait_ge(load["b2p2"], 16)
            diag = b2p2_sb[:, :, :].rearrange("p k (t c) -> p (k t) c", c=P)[:, 0:5:4, :]
            nc.vector.tensor_tensor(diag, diag, two_idents, ALU.add).then_inc(b_ready, 1)
            for k in range(KT):
                p2 = b2p2_sb[:, k, D:D + R2].rearrange("p (f r) -> p f r", r=RANK)
                nc.vector.tensor_tensor(p2, p2, s2_all.unsqueeze(2).to_broadcast([P, NE2, RANK]),
                                        ALU.mult).then_inc(p2_scaled, 1)
            dve.wait_ge(load["wb"], 16)
            diag = b1T_sb[:, :, :].rearrange("p k (t c) -> p (k t) c", c=P)[:, 0:4:3, :]
            nc.vector.tensor_tensor(diag, diag, two_idents, ALU.add).then_inc(b_ready, 1)
            dve.wait_ge(chosen_ready, 3)
            adapters = {g: registers(dve, ID2, g * BG, BG) for g in PICKED_BY_DVE}
            for k in range(KT):
                dve.wait_ge(bp_done, k + 1)
                nc.vector.tensor_copy(p2_all[:, 1 + k, :], bp_ps[k][:, D:D + R2]).then_inc(b1p2_ready, 1)
                nc.vector.tensor_copy(b12_hi[:, k, :], bp_ps[k][:, 0:D]).then_inc(b12_hi_ready, 1)
                dve.wait_ge(x_hi_ready, k + 1)
                nc.vector.tensor_tensor(x_lo[:, k, :], xT_sb[:, k, :], x_hi[:, k, :],
                                        ALU.subtract).then_inc(x_lo_ready, 1)
                dve.wait_ge(b12_hi_ready, k + 1)
                nc.vector.tensor_tensor(b12_lo[:, k, :], bp_ps[k][:, 0:D], b12_hi[:, k, :],
                                        ALU.subtract).then_inc(b12_lo_ready, 1)
            dve.wait_ge(mask_ready, 1)
            dve.wait_ge(z1_done, 1)
            for par in (EVEN, ODD):
                nc.vector.tensor_tensor(
                    z[par][Z1[par], :, :].rearrange("p j (q c) -> p j q c", q=BG),
                    z1_ps[Z1[par], :].rearrange("p (j q c) -> p j q c", j=PAIRS, q=BG),
                    mask1[Z1[par], :, par, :].unsqueeze(3).to_broadcast([H, PAIRS, BG, C]),
                    ALU.mult).then_inc(z1_ready, 1)
            dve.wait_ge(b1p2_ready, KT)
            dve.wait_ge(q1p2_ready, 2)
            dve.wait_ge(p2_zeroed, 2)
            for g in PICKED_BY_DVE:
                for copied in pick_p2(nc.vector.tensor_copy, g, adapters[g]):
                    copied.then_inc(picked[g], 1)
            dve.wait_ge(z_zeroed, 2)
            def layer0_residual(g):
                dve.wait_ge(load_w0[g], 16 * BG)
                whole = w0_bd[:, g, :, :].rearrange("p q c -> p (q c)")
                nc.vector.tensor_tensor(whole, whole, ident[:, :], ALU.add).then_inc(w0_ready, 1)

            dve.wait_ge(load["q2"], 16 * PAIRS)
            nc.vector.tensor_copy(qq[EVEN][Z2[EVEN], :, :], q2_pair[Z2[EVEN], :, :]).then_inc(q2_even_ready, 1)
            for n in range(2):
                dve.wait_ge(z2_done, n + 1)
                for par in (EVEN, ODD):
                    nc.vector.tensor_tensor(
                        z[par][Z2[par], 2 * n:2 * n + 2, :].rearrange("p j (q c) -> p j q c", q=BG),
                        z2_ps[n][Z2[par], 0:2 * P].rearrange("p (j q c) -> p j q c", j=2, q=BG),
                        in_block[Z2[par], :].unsqueeze(1).unsqueeze(3).to_broadcast([H, 2, BG, C]),
                        ALU.mult).then_inc(z2_ready, 1)
                if n == 0:
                    for g in range(EARLY0):
                        layer0_residual(g)
            experts = {g: registers(dve, ID3, g * BG, BG) for g in range(G3_DVE)}
            for g in range(EARLY0, BEFORE3):
                layer0_residual(g)
            for n in range(LOADS3_POOL, LOADS3):
                dve.wait_ge(load_w3[n], 16)
                for e in range(n * EL, (n + 1) * EL):
                    layer3_residual(nc.vector, e).then_inc(w3_last_ready, 1)

            def copy_group_experts(g):
                for copied in copy_experts(nc.vector.tensor_copy, g, experts[g]):
                    copied.then_inc(w3_copied, 1)

            dve.wait_ge(w3_ready, LOADS3_POOL * EL)
            dve.wait_ge(w3_last_ready, NE3 - LOADS3_POOL * EL)
            for g in range(BEFORE3, G):
                copy_group_experts(g - BEFORE3)
                layer0_residual(g)
            copy_group_experts(G - BEFORE3)
            for g in range(G):
                dve.wait_ge(load_bias[g], 16)
                dve.wait_ge(out_done, g + 1)
                nc.vector.tensor_tensor(out_sb[:, g, :], out_ps[g % len(out_ps)][:, 0:D], bias[:, g, :],
                                        ALU.add).then_inc(out_ready, 1)
                ahead = G - BEFORE3 + 1 + g
                if ahead < G3_DVE:
                    copy_group_experts(ahead)

        @block.tensor
        def _(pe):
            mm = nc.tensor.matmul

            pe.wait_ge(zeros_ready, 1)
            for _ in range(WARM_UP):
                mm(z2_ps[0][:, 0:2 * P], zeros[:, 0:P], zeros[:, 0:2 * P], start=True, stop=True)

            pe.wait_ge(load["wt_ab"], 16)
            for k in range(KT):
                for j in range(KT):
                    last = mm(p1_ps[:, k, :], wt_ab_sb[:, j, tile(k)], wt_ab_sb[:, j, D:], start=j == 0, stop=j == KT - 1)
            last.then_inc(p1_done, 1)
            pe.wait_ge(load["wpT"], 16)
            for k in range(KT):
                for j in range(KT):
                    last = mm(q1T_ps[:, k, :], wpT_sb[:, j, tile(k)], wt_ab_sb[:, j, D:], start=j == 0, stop=j == KT - 1)
            last.then_inc(q1_done, 1)

            pe.wait_ge(b_ready, 2)
            pe.wait_ge(p2_scaled, KT)
            for k in range(KT):
                for j in range(KT):
                    last = mm(bp_ps[k][:, 0:D + R2], b1T_sb[:, j, tile(k)], b2p2_sb[:, j, :],
                              start=j == 0, stop=j == KT - 1)
                last.then_inc(bp_done, 1)
            pe.wait_ge(q1_ready, 1)
            for j in range(KT):
                for half in (slice(0, H), slice(H, P)):
                    last = mm(qb_ps[half, 0:D + R2], q1T[:, j, :], b2p2_sb[:, j, :], start=j == 0, stop=j == KT - 1)
            last.then_inc(qb_done, 1)

            pe.wait_ge(p1_ready, 1)
            pe.wait_ge(load["x0"], 16)
            pe.wait_ge(load["x1"], 16)
            for k in range(KT):
                xT_pairs = xT_sb[:, k, :].rearrange("p (j e r) -> p j e r", j=PAIRS, e=2)
                for par in (EVEN, ODD):
                    last = mm(z1_ps[Z1[par], :].rearrange("p (j r) -> p j r", j=PAIRS), p1[:, k, :],
                              xT_pairs[:, :, par, :], start=k == 0, stop=k == KT - 1)
            last.then_inc(z1_done, 1)

            def y_from_x(g):
                if g >= len(y_ps):
                    pe.wait_ge(y_ready, g + 1 - len(y_ps))
                for k in range(KT):
                    for x_part, b_part in ((x_hi, b12_hi), (x_lo, b12_hi), (x_hi, b12_lo)):
                        mm(y_ps[g % len(y_ps)][:, 0:D], x_part[:, k, rows(g)], b_part[:, k, :],
                           start=k == 0 and x_part is x_hi and b_part is b12_hi, stop=False)

            def y_from_z(g):
                j, par = divmod(g, 2)
                pe.wait_ge(z2_ready, 2 * (j // 2) + par + 1)
                mm(y_ps[g % len(y_ps)][:, 0:D], z[par][:, j, :], qq[par][:, j, :], start=False, stop=True).then_inc(y_done, 1)

            def z2_of(j):
                for g in (2 * j, 2 * j + 1):
                    pe.wait_ge(picked[g], BG)
                ps = {par: z2_ps[j // 2][Z2[par], (j % 2) * P:(j % 2 + 1) * P] for par in (EVEN, ODD)}
                for k in range(KT):
                    for par in (EVEN, ODD):
                        mm(ps[par], p2_of[:, 2 * j + par, B1P2[par][k], :], xT_sb[:, k, rows(2 * j + par)],
                           start=k == 0, stop=False)
                pe.wait_ge(z1_ready, 2)
                pe.wait_ge(z_zeroed, 2)
                for par in (EVEN, ODD):
                    last = mm(ps[par], p2_of[:, 2 * j + par, Q1P2[par], :], z[par][:, j, :], start=False, stop=True)
                return last

            def mix(g):
                pe.wait_ge(y_ready, g + 1)
                pe.wait_ge(w0_ready, g + 1)
                if g >= 2:
                    pe.wait_ge(mix_ready, g - 1)
                for k in range(KT):
                    last = mm(mix_ps[g % 2][:, tile(k)], y_sb[:, g, tile(k)],
                              w0_bd[:, g, :, :].rearrange("p q c -> p (q c)"), start=True, stop=True)
                last.then_inc(mix_done, 1)

            pe.wait_ge(x_hi_ready, KT)
            pe.wait_ge(x_lo_ready, KT)
            pe.wait_ge(b12_hi_ready, KT)
            pe.wait_ge(b12_lo_ready, KT)
            for g in range(len(y_ps)):
                y_from_x(g)
            for j in range(PAIRS):
                last = z2_of(j)
                if j % 2:
                    last.then_inc(z2_done, 1)
            pe.wait_ge(q2_even_ready, 1)
            pe.wait_ge(q1b2_ready, 2)
            y_from_z(0)
            pe.wait_ge(q2_odd_ready, 1)
            y_from_z(1)
            y_from_z(2)
            mix(0)
            for g in range(3, G):
                mix(g - 2)
                y_from_x(g)
                y_from_z(g)
            mix(G - 2)

            for g in range(G):
                if g == 2:
                    mix(G - 1)
                pe.wait_ge(mix_ready, g + 1)
                if g < G3_DVE:
                    pe.wait_ge(w3_copied, (g + 1) * BG)
                else:
                    pe.wait_ge(w3_copied_last, (g + 1 - G3_DVE) * BG)
                if g >= len(out_ps):
                    pe.wait_ge(out_ready, g + 1 - len(out_ps))
                for k in range(KT):
                    for q in range(BG):
                        last = mm(out_ps[g % len(out_ps)][q * C:(q + 1) * C, 0:D], x2T[:, g, k, q * C:(q + 1) * C],
                                  w3_of[:, g * BG + q, k, :], start=k == 0, stop=k == KT - 1)
                last.then_inc(out_done, 1)


def kernel(x, itok_B_1_198, itok_B_0_3, itok_B_0_6, itok_B_0_15, L0_cond_weights, L1_cond_W_base, L1_cond_Wt,
           L1_cond_A, L1_cond_B_w, L1_cond_Wp, L1_cond_scaling, L2_cond_W, L2_cond_A, L2_cond_Bm,
           L2_cond_scalings, L3_cond_W, L3_cond_b):
    import numpy as np
    import concourse.bacc as bacc
    from concourse.bass_utils import run_bass_kernel_spmd

    def tiled(a):
        return a.reshape(KT, P, -1).transpose(1, 0, 2)

    def by_group(ids):
        return np.repeat(ids.reshape(G, BG), C, axis=1).T

    x, w0, w3 = np.asarray(x), np.asarray(L0_cond_weights), np.asarray(L3_cond_W)
    id0, id1, id2, id3 = (np.asarray(a) for a in (itok_B_1_198, itok_B_0_3, itok_B_0_6, itok_B_0_15))
    id2_of_row = np.repeat(id2.reshape(PAIRS, 2 * BG), RANK, axis=1).T
    ids = np.concatenate([np.broadcast_to(np.concatenate([id0, id1, id2, id3]), (P, 4 * B)),
                          id2_of_row, by_group(id3)], axis=1)
    s1, s2 = np.asarray(L1_cond_scaling), np.asarray(L2_cond_scalings)
    s1_s2 = np.concatenate([np.tile(np.repeat(s1, RANK), P // R1)[:, None], np.broadcast_to(s2, (P, NE2))], axis=1)
    p = np.arange(P)[:, None]
    blocks = np.concatenate([p % H // RANK, p % RANK, p % H // RANK == np.arange(BG)], axis=1).astype(np.float32)
    a1T = np.asarray(L1_cond_A).reshape(R1, D).T
    bwT = np.asarray(L1_cond_B_w).transpose(1, 0, 2).reshape(D, R1)
    p2 = np.asarray(L2_cond_A).reshape(R2, D).T
    feeds = {
        "xT": tiled(x.reshape(ROWS, D).T),
        "wt_ab": tiled(np.concatenate([np.asarray(L1_cond_Wt), a1T, bwT], axis=1)),
        "wpT": tiled(np.asarray(L1_cond_Wp).T),
        "wb": tiled(np.asarray(L1_cond_W_base)),
        "b2p2": tiled(np.concatenate([np.asarray(L2_cond_W).T, p2], axis=1)),
        "q2": np.asarray(L2_cond_Bm).transpose(0, 2, 1).reshape(R2, D),
        "small": np.concatenate([s1_s2, blocks], axis=1),
        "ids": ids,
        "w0": w0,
        "w3": w3.reshape(NE3, KT, P, D).transpose(2, 0, 1, 3),
        "b3": np.asarray(L3_cond_b),
    }
    feeds = {n: np.ascontiguousarray(a) for n, a in feeds.items()}
    nc = bacc.Bacc("TRN2", target_bir_lowering=False, num_devices=1)
    args = [nc.dram_tensor(n, a.shape, mybir.dt.from_np(a.dtype), kind="ExternalInput").ap()
            for n, a in feeds.items()]
    out = nc.dram_tensor("out", (ROWS, D), F32, kind="ExternalOutput").ap()
    cond_resid_kernel(nc, *args, out)
    got = run_bass_kernel_spmd(nc, [feeds], core_ids=[0]).results[0]["out"]
    return got.reshape(B, C, D)
```
